# Optimizing a Trainium2 kernel written in Bass

```python
import numpy as np
import jax
import jax.numpy as jnp

def _softmax(x, axis=-1):
    return jax.nn.softmax(x, axis=axis)

def _gelu(x):
    return jax.nn.gelu(x, approximate=True)

def _silu(x):
    return jax.nn.silu(x)

def _sigmoid(x):
    return jax.nn.sigmoid(x)

def _layernorm(x, axis=-1, eps=1e-05):
    m = jnp.mean(x, axis=axis, keepdims=True)
    v = jnp.var(x, axis=axis, keepdims=True)
    return (x - m) / jnp.sqrt(v + eps)

def _scatter_add(tgt, idx, src, axis=0):
    return tgt.at[idx].add(src)

def _segment_sum(src, seg, n):
    return jax.ops.segment_sum(src, seg, n)
kernel_name = 'mk_cond_seq_d2_seqx_r8_5b48ae'

def setup_inputs(seed: int=0):
    np.random.seed(seed)
    _w = jnp.asarray

    def _rec_inputs():
        import jax
        import jax.numpy as jnp
        _rk = jax.random.key(seed)
        x = -0.0002928 + 1 * jax.random.normal(jax.random.fold_in(_rk, 1), (32, 128, 128), jnp.float32)
        _lenS = 128 - jax.random.randint(jax.random.fold_in(_rk, 7), (32,), 0, max(1, 128 // 4) + 1, jnp.int32)
        _lenS2 = 128 - jax.random.randint(jax.random.fold_in(_rk, 8), (32,), 0, max(1, 128 // 4) + 1, jnp.int32)
        cond_1024 = 0.0061147 + 1.02565 * jax.random.normal(jax.random.fold_in(_rk, 11), (32, 128), jnp.float32)
        _validS = jnp.arange(128)[None, :] < _lenS[:, None]
        _validS2 = jnp.arange(128)[None, :] < _lenS2[:, None]
        _causal = jnp.tril(jnp.ones((128, 128), dtype=bool))
        mask_BxSxSx11_ik0 = jnp.where(jnp.ones((32, 128, 128, 11), dtype=bool), 0, 1).astype(jnp.int32)
        return (x, cond_1024, mask_BxSxSx11_ik0)
    x, cond_1024, mask_BxSxSx11_ik0 = _rec_inputs()

    def _L0_cond_setup():
        import jax, jax.numpy as jnp
        import numpy as np
        B, T, DIM = (4, 128, 128)
        COND = 128
        HEADS, DH = (16, 64)
        INNER = HEADS * DH
        MLP = 512
        EPS = 1e-05

        def _layernorm(x):
            mu = jnp.mean(x, axis=-1, keepdims=True)
            var = jnp.mean(jnp.square(x - mu), axis=-1, keepdims=True)
            return (x - mu) * jax.lax.rsqrt(var + EPS)

        def _modulate(x, shift, scale):
            return x * (1.0 + scale) + shift

        def _attention(x, W_qkv, W_out, b_out):
            Bq, Tq, _ = x.shape
            qkv = x @ W_qkv
            q, k, v = jnp.split(qkv, 3, axis=-1)
            q = q.reshape(Bq, Tq, HEADS, DH)
            k = k.reshape(Bq, Tq, HEADS, DH)
            v = v.reshape(Bq, Tq, HEADS, DH)
            scale = DH ** (-0.5)
            attn = jnp.einsum('bqhd,bkhd->bhqk', q, k) * scale
            attn = jax.nn.softmax(attn, axis=-1)
            out = jnp.einsum('bhqk,bkhd->bqhd', attn, v).reshape(Bq, Tq, INNER)
            return out @ W_out + b_out

        def _ff(x, W1, b1, W2, b2):
            return jax.nn.gelu(x @ W1 + b1, approximate=False) @ W2 + b2
        key = jax.random.key(seed)
        ks = jax.random.split(key, 12)
        s = 0.02
        return {'x': jax.random.normal(ks[0], (B, T, DIM), jnp.float32), 'c': jax.random.normal(ks[1], (B, 1, COND), jnp.float32), 'W_mod': jax.random.normal(ks[2], (COND, 6 * DIM), jnp.float32) * s, 'b_mod': jax.random.normal(ks[3], (6 * DIM,), jnp.float32) * s, 'W_qkv': jax.random.normal(ks[4], (DIM, 3 * INNER), jnp.float32) * s, 'W_out': jax.random.normal(ks[5], (INNER, DIM), jnp.float32) * s, 'b_out': jax.random.normal(ks[6], (DIM,), jnp.float32) * s, 'W1': jax.random.normal(ks[7], (DIM, MLP), jnp.float32) * s, 'b1': jax.random.normal(ks[8], (MLP,), jnp.float32) * s, 'W2': jax.random.normal(ks[9], (MLP, DIM), jnp.float32) * s, 'b2': jax.random.normal(ks[10], (DIM,), jnp.float32) * s}
    _L0_cond_all = _L0_cond_setup()
    _L0_cond_in = {k: v for k, v in _L0_cond_all.items() if k in ('W_mod', 'b_mod', 'W_qkv', 'W_out', 'b_out', 'W1', 'b1', 'W2', 'b2')}
    del _L0_cond_all

    def _L1_cond_setup():
        import jax, jax.numpy as jnp
        import numpy as np
        NONGT = 20
        H = 16
        NEG = -9000000000000000.0

        def _gat_attention(self_feat, cond_adj, label_bias, Wq, bq, Wk, bk, Wout, bout):
            B, N, F = self_feat.shape
            ng = min(NONGT, N)
            dh = F // H
            kv = self_feat[:, :ng]
            qh = (self_feat @ Wq.T + bq).reshape(B, N, H, dh)
            kh = (kv @ Wk.T + bk).reshape(B, ng, H, dh)
            aff = jnp.einsum('bnhd,bmhd->bnhm', qh, kh) * (1.0 / np.sqrt(dh))
            mask = cond_adj[:, :, None, :] > 0
            aff = jnp.where(mask, aff, NEG) + label_bias[:, :, None, :]
            w = jax.nn.softmax(aff, axis=-1)
            out_t = jnp.einsum('bnhm,bmf->bnhf', w, kv)
            out = jnp.einsum('bnhf,hgf->bnhg', out_t, Wout) + bout.reshape(H, F // H)
            return out.reshape(B, N, F)

        def _forward(v, q, adj, W_self, b_self, w_bias, b_bias, Wq, bq, Wk, bk, Wout, bout):
            adj_f = adj.astype(jnp.float32)
            exp_v = v
            row_zero = exp_v.sum(-1) == 0
            q_exp = jnp.where(row_zero[..., None], 0.0, q[:, None, :])
            vcq = jnp.concatenate([exp_v, q_exp], axis=-1)
            self_feat = vcq @ W_self.T + b_self
            output = self_feat
            for d in range(2):
                A = adj_f if d == 0 else jnp.swapaxes(adj_f, 1, 2)
                A = A[:, :, :NONGT, :]
                cond = A.sum(-1)
                vb = A @ w_bias + b_bias
                output = output + _gat_attention(self_feat, cond, vb, Wq[d], bq[d], Wk[d], bk[d], Wout[d], bout[d])
            rel = jax.nn.relu(output)
            return exp_v + rel
        key = jax.random.key(seed)
        ks = jax.random.split(key, 8)
        B, N, L, F, Q = (32, 36, 11, 128, 128)
        IN = F + Q
        s = 0.02
        return {'v': jax.random.normal(ks[0], (B, N, F), jnp.float32), 'q': jax.random.normal(ks[1], (B, Q), jnp.float32), 'adj': jax.random.randint(ks[2], (B, N, N, L), 0, 2, jnp.int32), 'W_self': jax.random.normal(ks[3], (F, IN), jnp.float32) * s, 'b_self': jnp.zeros((F,), jnp.float32), 'w_bias': jax.random.normal(ks[4], (L,), jnp.float32) * s, 'b_bias': jnp.zeros((), jnp.float32), 'Wq': jax.random.normal(ks[5], (2, F, F), jnp.float32) * s, 'bq': jnp.zeros((2, F), jnp.float32), 'Wk': jax.random.normal(ks[6], (2, F, F), jnp.float32) * s, 'bk': jnp.zeros((2, F), jnp.float32), 'Wout': jax.random.normal(ks[7], (2, H, F // H, F), jnp.float32) * s, 'bout': jnp.zeros((2, F), jnp.float32)}
    _L1_cond_all = _L1_cond_setup()
    _L1_cond_in = {k: v for k, v in _L1_cond_all.items() if k in ('W_self', 'b_self', 'w_bias', 'b_bias', 'Wq', 'bq', 'Wk', 'bk', 'Wout', 'bout')}
    del _L1_cond_all
    return {'x': x, 'cond_1024': cond_1024, 'mask_BxSxSx11_ik0': mask_BxSxSx11_ik0, 'L0_cond_W_mod': _L0_cond_in['W_mod'], 'L0_cond_b_mod': _L0_cond_in['b_mod'], 'L0_cond_W_qkv': _L0_cond_in['W_qkv'], 'L0_cond_W_out': _L0_cond_in['W_out'], 'L0_cond_b_out': _L0_cond_in['b_out'], 'L0_cond_W1': _L0_cond_in['W1'], 'L0_cond_b1': _L0_cond_in['b1'], 'L0_cond_W2': _L0_cond_in['W2'], 'L0_cond_b2': _L0_cond_in['b2'], 'L1_cond_W_self': _L1_cond_in['W_self'], 'L1_cond_b_self': _L1_cond_in['b_self'], 'L1_cond_w_bias': _L1_cond_in['w_bias'], 'L1_cond_b_bias': _L1_cond_in['b_bias'], 'L1_cond_Wq': _L1_cond_in['Wq'], 'L1_cond_bq': _L1_cond_in['bq'], 'L1_cond_Wk': _L1_cond_in['Wk'], 'L1_cond_bk': _L1_cond_in['bk'], 'L1_cond_Wout': _L1_cond_in['Wout'], 'L1_cond_bout': _L1_cond_in['bout']}

def reference(x, cond_1024, mask_BxSxSx11_ik0, L0_cond_W_mod, L0_cond_b_mod, L0_cond_W_qkv, L0_cond_W_out, L0_cond_b_out, L0_cond_W1, L0_cond_b1, L0_cond_W2, L0_cond_b2, L1_cond_W_self, L1_cond_b_self, L1_cond_w_bias, L1_cond_b_bias, L1_cond_Wq, L1_cond_bq, L1_cond_Wk, L1_cond_bk, L1_cond_Wout, L1_cond_bout):
    import jax
    import jax.numpy as jnp

    def _L0_cond_ref(x, c, W_mod, b_mod, W_qkv, W_out, b_out, W1, b1, W2, b2):
        import jax, jax.numpy as jnp
        import numpy as np
        B, T, DIM = (4, 128, 128)
        COND = 128
        HEADS, DH = (16, 64)
        INNER = HEADS * DH
        MLP = 512
        EPS = 1e-05

        def _layernorm(x):
            mu = jnp.mean(x, axis=-1, keepdims=True)
            var = jnp.mean(jnp.square(x - mu), axis=-1, keepdims=True)
            return (x - mu) * jax.lax.rsqrt(var + EPS)

        def _modulate(x, shift, scale):
            return x * (1.0 + scale) + shift

        def _attention(x, W_qkv, W_out, b_out):
            Bq, Tq, _ = x.shape
            qkv = x @ W_qkv
            q, k, v = jnp.split(qkv, 3, axis=-1)
            q = q.reshape(Bq, Tq, HEADS, DH)
            k = k.reshape(Bq, Tq, HEADS, DH)
            v = v.reshape(Bq, Tq, HEADS, DH)
            scale = DH ** (-0.5)
            attn = jnp.einsum('bqhd,bkhd->bhqk', q, k) * scale
            attn = jax.nn.softmax(attn, axis=-1)
            out = jnp.einsum('bhqk,bkhd->bqhd', attn, v).reshape(Bq, Tq, INNER)
            return out @ W_out + b_out

        def _ff(x, W1, b1, W2, b2):
            return jax.nn.gelu(x @ W1 + b1, approximate=False) @ W2 + b2
        mod = jax.nn.silu(c) @ W_mod + b_mod
        sh_msa, sc_msa, g_msa, sh_mlp, sc_mlp, g_mlp = jnp.split(mod, 6, axis=-1)
        x = x + g_msa * _attention(_modulate(_layernorm(x), sh_msa, sc_msa), W_qkv, W_out, b_out)
        x = x + g_mlp * _ff(_modulate(_layernorm(x), sh_mlp, sc_mlp), W1, b1, W2, b2)
        return x

    def _L1_cond_ref(v, q, adj, W_self, b_self, w_bias, b_bias, Wq, bq, Wk, bk, Wout, bout):
        import jax, jax.numpy as jnp
        import numpy as np
        NONGT = 20
        H = 16
        NEG = -9000000000000000.0

        def _gat_attention(self_feat, cond_adj, label_bias, Wq, bq, Wk, bk, Wout, bout):
            B, N, F = self_feat.shape
            ng = min(NONGT, N)
            dh = F // H
            kv = self_feat[:, :ng]
            qh = (self_feat @ Wq.T + bq).reshape(B, N, H, dh)
            kh = (kv @ Wk.T + bk).reshape(B, ng, H, dh)
            aff = jnp.einsum('bnhd,bmhd->bnhm', qh, kh) * (1.0 / np.sqrt(dh))
            mask = cond_adj[:, :, None, :] > 0
            aff = jnp.where(mask, aff, NEG) + label_bias[:, :, None, :]
            w = jax.nn.softmax(aff, axis=-1)
            out_t = jnp.einsum('bnhm,bmf->bnhf', w, kv)
            out = jnp.einsum('bnhf,hgf->bnhg', out_t, Wout) + bout.reshape(H, F // H)
            return out.reshape(B, N, F)

        def _forward(v, q, adj, W_self, b_self, w_bias, b_bias, Wq, bq, Wk, bk, Wout, bout):
            adj_f = adj.astype(jnp.float32)
            exp_v = v
            row_zero = exp_v.sum(-1) == 0
            q_exp = jnp.where(row_zero[..., None], 0.0, q[:, None, :])
            vcq = jnp.concatenate([exp_v, q_exp], axis=-1)
            self_feat = vcq @ W_self.T + b_self
            output = self_feat
            for d in range(2):
                A = adj_f if d == 0 else jnp.swapaxes(adj_f, 1, 2)
                A = A[:, :, :NONGT, :]
                cond = A.sum(-1)
                vb = A @ w_bias + b_bias
                output = output + _gat_attention(self_feat, cond, vb, Wq[d], bq[d], Wk[d], bk[d], Wout[d], bout[d])
            rel = jax.nn.relu(output)
            return exp_v + rel
        return _forward(v, q, adj, W_self, b_self, w_bias, b_bias, Wq, bq, Wk, bk, Wout, bout)
    x = _L0_cond_ref(x, cond_1024[:, None, :], L0_cond_W_mod, L0_cond_b_mod, L0_cond_W_qkv, L0_cond_W_out, L0_cond_b_out, L0_cond_W1, L0_cond_b1, L0_cond_W2, L0_cond_b2)
    x = _L1_cond_ref(x, cond_1024, mask_BxSxSx11_ik0, L1_cond_W_self, L1_cond_b_self, L1_cond_w_bias, L1_cond_b_bias, L1_cond_Wq, L1_cond_bq, L1_cond_Wk, L1_cond_bk, L1_cond_Wout, L1_cond_bout)
    return x

_drawn_inputs = setup_inputs


def setup_inputs(seed=0):
    import zlib

    import numpy as np

    out = dict(_drawn_inputs(seed))
    spreads = {'L1_cond_b_self': (0.0, 0.8),
     'L1_cond_bq': (0.0, 0.1),
     'L1_cond_bk': (0.0, 0.1),
     'L1_cond_bout': (0.0, 0.8)}
    factors = {'L0_cond_W_mod': 6.212,
     'L0_cond_b_mod': 8.0,
     'L0_cond_W_qkv': 8.0,
     'L0_cond_W_out': 8.0,
     'L0_cond_b_out': 36.439,
     'L0_cond_W1': 7.796,
     'L0_cond_b1': 8.0,
     'L0_cond_W2': 7.642,
     'L0_cond_b2': 37.251}
    for name, (base, spread) in spreads.items():
        noise = np.random.default_rng([zlib.crc32(name.encode()), seed]).standard_normal(out[name].shape)
        drawn = base * np.exp(spread * noise) if base else spread * noise
        out[name] = jnp.asarray(drawn.astype(out[name].dtype))
    for name, factor in factors.items():
        out[name] = (out[name] * factor).astype(out[name].dtype)
    return out
```

```python
import numpy as np
import concourse.bass as bass
from concourse import mybir
from contextlib import ExitStack

B, T, D = 32, 128, 128
PAIRS = B // 2
HEADS, DH = 16, 64
INNER = HEADS * DH
CHUNKS = INNER // 128
MLP = 512
MCH = MLP // 128
EPS = 1e-5
QSCALE = DH ** -0.5
NG = 20
L = 11
GH, GD = 16, 8
GSCALE = float(GD) ** -0.5
NEG = -9000000000000000.0
ROWS = 5
COLS = 4

F32 = mybir.dt.float32
F32R = mybir.dt.float32r
I32 = mybir.dt.int32
ALU = mybir.AluOpType
ACT = mybir.ActivationFunctionType
AX = mybir.AxisListType


class Kept:
    pass


class Step:

    def __init__(self, half, par):
        self.half, self.par, self.n = half, par, half * 2 + par


def zero_wait(eng, s, value):
    if not isinstance(value, int) or value > 0:
        eng.wait_ge(s, value)


def setup_phase(nc, g, a):
    with ExitStack() as ctx:
        def sb(name, shape, dt=F32):
            return ctx.enter_context(nc.sbuf_tensor(name, shape, dt))

        def sem(name):
            return ctx.enter_context(nc.semaphore(name))

        cT = sb("cT_sb", [128, B])
        sigT = sb("sigT", [128, B])
        siluT = sb("siluT", [128, B])
        w_mod = sb("w_mod_sb", [128, 6, 128])
        b_modT = sb("b_modT_sb", [128, 6])
        b_mod = sb("b_mod_rows", [B, 6, 128])
        b_out = sb("b_out_rows", [B, 128])
        b2 = sb("b2_rows", [B, 128])
        w_raw = sb("w_qkv_raw", [128, 3 * INNER])
        w1_raw = sb("w1_raw", [128, MLP])
        rows = sb("rows_sb", [B, ROWS, 128])
        col_ps = g.bank[0][:, 0:COLS * B].rearrange("p (j b) -> p j b", j=COLS)
        row_ps = g.bank[1][0:B, 0:384].rearrange("p (j f) -> p j f", j=3)

        cond_loaded = sem("cond_loaded")
        wmod_loaded = sem("wmod_loaded")
        wqkv_loaded = [sem(f"wqkv_loaded{n}") for n in range(6)]
        small_loaded = sem("small_loaded")
        kept_loaded = sem("kept_loaded")
        sig_exp = sem("sig_exp")
        silu_steps = sem("silu_steps")
        mods_ready = sem("mods_ready")
        row_steps = sem("row_steps")
        rows_stored = sem("rows_stored")
        hi_ready = sem("hi_ready")
        lo_ready = sem("lo_ready")
        ident_steps = sem("ident_steps")

        COL_OF = (0, 1, 3, 4)
        SPLIT = 512

        block = ctx.enter_context(nc.Block())

        @block.sync
        def _(sp):
            sp.dma_start(cT[:], a["cT"]).then_inc(cond_loaded, 16)
            sp.dma_start(w_mod[:], a["w_mod"].rearrange("p (j f) -> p j f", j=6)).then_inc(wmod_loaded, 16)
            for n in range(6):
                sp.dma_start(w_raw[:, n * SPLIT:(n + 1) * SPLIT],
                             a["w_qkv"][:, n * SPLIT:(n + 1) * SPLIT]).then_inc(wqkv_loaded[n], 16)
            sp.wait_ge(row_steps, ROWS)
            sp.dma_start(g.rows_d, rows[:]).then_inc(rows_stored, 16)
            sp.wait_ge(rows_stored, 16)
            sp.wait_ge(kept_loaded, 16 * 12)

        @block.gpsimd
        def _(pool):
            small = [(b_modT[:], a["b_modT"]), (b_mod[:], a["b_mod"].rearrange("(j f) -> j f", j=6).partition_broadcast(B)),
                     (b_out[:], a["b_out"].partition_broadcast(B)), (b2[:], a["b2"].partition_broadcast(B)),
                     (w1_raw[:], a["w1"])]
            for dst, src in small:
                pool.dma_start(dst, src).then_inc(small_loaded, 16)
            pool.dma_start(g.w_self[:], a["w_selfT"].rearrange("(j p) f -> p j f", j=2)).then_inc(kept_loaded, 16)
            kept = [(g.w_out[:], a["w_out"].rearrange("(c p) f -> p c f", c=CHUNKS)),
                    (g.b1T[:], a["b1T"]), (g.w2[:], a["w2"].rearrange("(c p) f -> p c f", c=MCH)),
                    (g.gqk_w[:], a["gqkT"]), (g.gqk_b[:], a["gbT"]), (g.gout_w[:], a["w_goutT"]),
                    (g.b_self[:], a["b_self"].partition_broadcast(128)),
                    (g.b_gout[:], a["b_gout"].partition_broadcast(128)),
                    (g.w_bias[:], a["w_bias"].partition_broadcast(128)),
                    (g.b_bias[:], a["b_bias"].partition_broadcast(128)),
                    (g.blockmask[:], a["blockmask"])]
            for dst, src in kept:
                pool.dma_start(dst, src).then_inc(kept_loaded, 16)
            pool.memset(g.ident[:], 0.0).then_inc(ident_steps, 1)
            pool.wait_ge(ident_steps, 1)
            pool.affine_select(out=g.ident[:], in_=g.ident[:], compare_op=ALU.not_equal, fill=1.0, base=0,
                               pattern=[[-1, 128]], channel_multiplier=1).then_inc(ident_steps, 1)

        @block.scalar
        def _(act):
            act.wait_ge(cond_loaded, 16)
            act.activation(sigT[:], cT[:], ACT.Exp, scale=-1.0).then_inc(sig_exp, 1)
            for n in range(6):
                act.wait_ge(wqkv_loaded[n], 16)
                cols = slice(n * SPLIT, (n + 1) * SPLIT)
                act.activation(g.wq_hi[:, cols], w_raw[:, cols], ACT.Copy,
                               scale=QSCALE if n < 2 else 1.0).then_inc(hi_ready, 1)
            act.wait_ge(small_loaded, 16 * 5)
            act.activation(g.w1_hi[:], w1_raw[:], ACT.Copy).then_inc(hi_ready, 1)

        @block.vector
        def _(dve):
            dve.wait_ge(sig_exp, 1)
            dve.tensor_scalar(sigT[:], sigT[:], 1.0, None, ALU.add).then_inc(silu_steps, 1)
            dve.wait_ge(silu_steps, 1)
            dve.reciprocal(siluT[:], sigT[:]).then_inc(silu_steps, 1)
            dve.wait_ge(silu_steps, 2)
            dve.tensor_tensor(siluT[:], siluT[:], cT[:], ALU.mult).then_inc(silu_steps, 1)
            dve.wait_ge(mods_ready, 1)
            dve.wait_ge(small_loaded, 16 * 5)
            for n, j in enumerate(COL_OF):
                dve.tensor_scalar(g.modT[:, :, n], col_ps[:, n, :], b_modT[:, j:j + 1], float(n % 2),
                                  ALU.add, ALU.add)
            for n, j in ((0, 2), (2, 5)):
                dve.tensor_tensor(rows[:, n, :], row_ps[:, n // 2, :], b_mod[:, j, :],
                                  ALU.add).then_inc(row_steps, 1)
            dve.tensor_copy(rows[:, 4, :], row_ps[:, 2, :]).then_inc(row_steps, 1)
            dve.wait_ge(row_steps, 3)
            dve.tensor_tensor(rows[:, 1, :], rows[:, 0, :], b_out[:], ALU.mult).then_inc(row_steps, 1)
            dve.tensor_tensor(rows[:, 3, :], rows[:, 2, :], b2[:], ALU.mult).then_inc(row_steps, 1)
            for n in range(6):
                cols = slice(n * SPLIT, (n + 1) * SPLIT)
                dve.wait_ge(hi_ready, n + 1)
                dve.scalar_tensor_tensor(out=g.wq_lo[:, cols], in0=w_raw[:, cols],
                                         scalar=QSCALE if n < 2 else 1.0,
                                         in1=g.wq_hi[:, cols].bitcast(F32),
                                         op0=ALU.mult, op1=ALU.subtract).then_inc(lo_ready, 1)
            dve.wait_ge(hi_ready, 7)
            dve.tensor_tensor(g.w1_lo[:], w1_raw[:], g.w1_hi[:].bitcast(F32), ALU.subtract).then_inc(lo_ready, 1)

        @block.tensor
        def _(pe):
            pe.wait_ge(silu_steps, 3)
            pe.wait_ge(wmod_loaded, 16)
            for n, j in enumerate(COL_OF):
                pe.matmul(col_ps[:, n, :], w_mod[:, j, :], siluT[:], start=True, stop=True)
            for n, j in enumerate((2, 5)):
                pe.matmul(row_ps[:, n, :], siluT[:], w_mod[:, j, :], start=True, stop=True)
            pe.wait_ge(kept_loaded, 16 * 12)
            pe.matmul(row_ps[:, 2, :], cT[:], g.w_self[:, 1, :], start=True, stop=True).then_inc(mods_ready, 1)


def attention_phase(nc, g):
    with ExitStack() as ctx:
        def sb(name, shape, dt=F32):
            return ctx.enter_context(nc.sbuf_tensor(name, shape, dt))

        def sem(name):
            return ctx.enter_context(nc.semaphore(name))

        x_in = sb("x_in", [128, 2, D])
        gate = sb("gate_msa", [128, 2, D])
        gate_b = sb("gate_b_out", [128, 2, D])
        x_gb = sb("x_gb", [128, 2, D])
        stats = sb("ln_stats", [128, 2, 6])
        meanvar = sb("ln_meanvar", [128, 2, 2])
        rstd = sb("ln_rstd", [128, 2])
        ln_const = sb("ln_const", [128, 2, 2])
        xhat = sb("xhat", [128, 2, D])
        shsc = sb("shift_scale", [128, 2, COLS])
        xT = sb("xT_mod", [128, 2, T])
        xT_hi = sb("xT_hi", [128, 2 * T], F32R)
        xT_lo = sb("xT_lo", [128, 2 * T], F32R)
        qk = sb("qk", [128, CHUNKS, 2, 2, T])
        v = sb("v", [128, 2, INNER])
        neg_max = sb("neg_max", [128, 2, 8])
        p = sb("p", [128, 2, 8, T])
        p_sum = sb("p_sum", [128, 2, 8])
        p_rsum = sb("p_rsum", [128, 2, 8])
        pT = sb("pT", [128, 8, T])
        oT = sb("oT", [128, 2, CHUNKS, T])
        gated = sb("gated", [128, 2, D])
        x1 = sb("x1", [128, 2, D])

        s_ps = [g.bank[n][:].rearrange("p (e j k) -> p e j k", e=2, j=4) for n in range(2)]
        t_ps = [g.bank[2][:, 512 * n:512 * n + 512] for n in range(2)]
        proj_ps = [g.bank[3][:, 512 * n:512 * n + 512] for n in range(2)]

        x_loaded = sem("x_loaded")
        gate_loaded = sem("gate_loaded")
        gate_b_loaded = sem("gate_b_loaded")
        x1_stored = sem("x1_stored")
        ln_stats_made = sem("ln_stats_made")
        ln_var_eps = sem("ln_var_eps")
        ln_const_set = sem("ln_const_set")
        ln_rstd_made = sem("ln_rstd_made")
        xhat_ready = sem("xhat_ready")
        x_gb_ready = sem("x_gb_ready")
        shsc_ready = sem("shsc_ready")
        xT_modulated = sem("xT_modulated")
        xT_split = sem("xT_split")
        proj_full = [sem(f"proj_full{n}") for n in range(2)]
        proj_saved = [sem(f"proj_saved{n}") for n in range(2)]
        scores_ready = sem("scores_ready")
        max_ready = sem("max_ready")
        exp_done = sem("exp_done")
        rsum_ready = sem("rsum_ready")
        p_ready = sem("p_ready")
        turn_full = [sem(f"turn_full{n}") for n in range(2)]
        turn_saved = [sem(f"turn_saved{n}") for n in range(2)]
        gated_ready = sem("gated_ready")
        x1_ready = sem("x1_ready")

        QK1, V1, XT, QK0, V0, OUT = (0, 4, 6, 7, 11, 13)
        TASKS = 14

        def task_bank(i, k):
            n = (k + 1) % 2
            if isinstance(i, int) and i < 0:
                return n, (k - XT - (n == 0)) // 2 + 1
            left_out = 3 if isinstance(i, int) and i == PAIRS - 1 and k == OUT else 0
            return n, i * (TASKS // 2) + (3 + n + k // 2 + 1 - left_out)

        def wait_saved(eng, i, k):
            n, count = task_bank(i, k)
            eng.wait_ge(proj_saved[n], count)

        def wait_bank(eng, i, k):
            n, count = task_bank(i, k)
            zero_wait(eng, proj_saved[n], count - 1)

        block = ctx.enter_context(nc.Block())

        @block.sync
        def _(sp):
            def load_x(i):
                sp.dma_start(x_in[:], g.x_p[i]).then_inc(x_loaded, 16)

            def load_gate_b(i):
                sp.dma_start(gate_b[:], g.rows_p[i][:, 1, :].partition_broadcast(128)).then_inc(gate_b_loaded, 16)

            load_x(0)
            load_gate_b(0)
            with sp.Fori(0, PAIRS - 1) as i:
                sp.wait_ge(x_gb_ready, i + 1)
                sp.wait_ge(xhat_ready, i * 2 + 2)
                load_x(i + 1)
                load_gate_b(i + 1)

        @block.gpsimd
        def _(pool):
            def load_gate(i):
                pool.dma_start(gate[:], g.rows_p[i][:, 0, :].partition_broadcast(128)).then_inc(gate_loaded, 16)

            def rstd_of(i):
                pool.wait_ge(ln_stats_made, i * 4 + 4)
                pool.tensor_tensor(rstd[:], meanvar[:, :, 1], ln_const[:, 0], ALU.add).then_inc(ln_var_eps, 1)
                pool.wait_ge(ln_var_eps, i + 1)
                pool.tensor_tensor(rstd[:], rstd[:], ln_const[:, 1], ALU.pow).then_inc(ln_rstd_made, 1)

            def body(i, last):
                pool.wait_ge(gate_loaded, i * 16 + 16)
                pool.wait_ge(gate_b_loaded, i * 16 + 16)
                pool.tensor_tensor(x_gb[:], x_in[:], gate_b[:], ALU.add).then_inc(x_gb_ready, 1)
                if not last:
                    rstd_of(i + 1)
                pool.wait_ge(x1_ready, i + 1)
                pool.dma_start(g.x1_p[i], x1[:]).then_inc(x1_stored, 16)
                pool.wait_ge(x1_stored, i * 16 + 16)
                if not last:
                    load_gate(i + 1)

            load_gate(0)
            pool.memset(ln_const[:, 0], EPS).then_inc(ln_const_set, 1)
            pool.memset(ln_const[:, 1], -0.5).then_inc(ln_const_set, 1)
            pool.wait_ge(ln_const_set, 2)
            rstd_of(0)
            with pool.Fori(0, PAIRS - 1) as i:
                body(i, False)
            body(PAIRS - 1, True)

        @block.tensor
        def _(pe):
            def turn_x(i):
                n, _ = task_bank(i, XT)
                pe.wait_ge(xhat_ready, i * 2 + 4)
                wait_bank(pe, i, XT)
                for b in range(2):
                    last = pe.transpose(proj_ps[n][:, b * T:b * T + T], xhat[:, b, :], g.ident[:])
                last.then_inc(proj_full[n], 1)

            def project_qk(i, k, c):
                n, _ = task_bank(i, k)
                wait_bank(pe, i, k)
                for which in range(2):
                    dst = proj_ps[n][:, which * 256:which * 256 + 256]
                    cols = slice(which * INNER + c * 128, which * INNER + c * 128 + 128)
                    pe.matmul(dst, g.wq_hi[:, cols], xT_hi[:], start=True, stop=False)
                    pe.matmul(dst, g.wq_hi[:, cols], xT_lo[:], start=False, stop=False)
                    last = pe.matmul(dst, g.wq_lo[:, cols], xT_hi[:], start=False, stop=True)
                last.then_inc(proj_full[n], 1)

            def project_v(i, k, half, b):
                n, _ = task_bank(i, k)
                wait_bank(pe, i, k)
                cols = slice(2 * INNER + half * 512, 2 * INNER + half * 512 + 512)
                toks = slice(b * T, b * T + T)
                pe.matmul(proj_ps[n], xT_hi[:, toks], g.wq_hi[:, cols], start=True, stop=False)
                pe.matmul(proj_ps[n], xT_hi[:, toks], g.wq_lo[:, cols], start=False, stop=False)
                pe.matmul(proj_ps[n], xT_lo[:, toks], g.wq_hi[:, cols], start=False,
                          stop=True).then_inc(proj_full[n], 1)

            def scores(i, unit, qk_body, qk_task):
                par, half, b = unit % 2, unit // 2 % 2, unit % 2
                wait_saved(pe, qk_body, qk_task + 2)
                wait_saved(pe, qk_body, qk_task + 3)
                zero_wait(pe, exp_done, i * 32 + (unit - 1) * 8)
                for j in range(4):
                    for e in range(2):
                        rows = slice(64 * e, 64 * e + 64)
                        c = 4 * half + j
                        last = pe.matmul(s_ps[par][:, e, j, :], qk[rows, c, 0, b, :], qk[rows, c, 1, b, :],
                                         start=True, stop=True)
                last.then_inc(scores_ready, 1)

            def turn_p(i, unit, grp):
                par = unit % 2
                pe.wait_ge(p_ready, i * 8 + (2 * unit + grp + 1))
                pe.wait_ge(turn_saved[grp], i * 8 + (2 * unit + 1) if grp == 0 else i * 4 + (unit + 1))
                for m in range(4):
                    last = pe.transpose(t_ps[grp][:, m * T:m * T + T], p[:, par, 4 * grp + m, :], g.ident[:])
                last.then_inc(turn_full[grp], 1)

            def probs_v(i, unit):
                half, b = unit // 2, unit % 2
                if half:
                    wait_saved(pe, i, V1 + b)
                else:
                    pe.wait_ge(proj_saved[b], i * (TASKS // 2) + (3 + b))
                pe.wait_ge(turn_saved[0], i * 8 + (2 * unit + 2))
                pe.wait_ge(turn_saved[1], i * 4 + (unit + 2))
                for j in range(4):
                    for e in range(2):
                        head = 8 * half + 2 * j + e
                        last = pe.matmul(t_ps[0][64 * e:64 * e + 64, j * T:j * T + T],
                                         v[:, b, head * DH:head * DH + DH], pT[:, 2 * j + e, :],
                                         start=True, stop=True)
                last.then_inc(turn_full[0], 1)

            def project_out(i, b):
                n, _ = task_bank(i, OUT)
                if b == 0:
                    wait_bank(pe, i, OUT)
                pe.wait_ge(turn_saved[0], i * 8 + (2 * (2 + b) + 3))
                for c in range(CHUNKS):
                    last = pe.matmul(proj_ps[n][:, b * D:b * D + D], oT[:, b, c, :], g.w_out[:, c, :],
                                     start=(c == 0), stop=(c == CHUNKS - 1))
                if b == 1:
                    last.then_inc(proj_full[n], 1)

            def first_half(i):
                pe.wait_ge(xT_split, i * 2 + 4)
                for j in range(4):
                    project_qk(i, QK0 + j, j)
                project_v(i, V0, 0, 0)
                project_v(i, V0 + 1, 0, 1)

            def body(i, last):
                project_qk(i, QK1, 4)
                turn_p(i, 0, 0)
                project_qk(i, QK1 + 1, 5)
                turn_p(i, 0, 1)
                project_qk(i, QK1 + 2, 6)
                probs_v(i, 0)
                project_qk(i, QK1 + 3, 7)

                scores(i, 2, i, QK1)
                project_v(i, V1, 1, 0)
                turn_p(i, 1, 0)
                project_v(i, V1 + 1, 1, 1)
                turn_p(i, 1, 1)
                if not last:
                    turn_x(i)
                probs_v(i, 1)

                scores(i, 3, i, QK1)
                if not last:
                    pe.wait_ge(xT_split, i * 2 + 4)
                    project_qk(i, QK0, 0)
                turn_p(i, 2, 0)
                if not last:
                    project_qk(i, QK0 + 1, 1)
                turn_p(i, 2, 1)
                if not last:
                    project_qk(i, QK0 + 2, 2)
                probs_v(i, 2)
                if not last:
                    project_qk(i, QK0 + 3, 3)

                    scores(i, 4, i, QK0)
                    project_v(i, V0, 0, 0)
                turn_p(i, 3, 0)
                if not last:
                    project_v(i, V0 + 1, 0, 1)
                turn_p(i, 3, 1)
                project_out(i, 0)
                probs_v(i, 3)
                if not last:
                    scores(i, 5, i, QK0)
                project_out(i, 1)

            turn_x(-1)
            first_half(-1)
            scores(0, 0, -1, QK0)
            scores(0, 1, -1, QK0)
            with pe.Fori(0, PAIRS - 1) as i:
                body(i, False)
            body(PAIRS - 1, True)

        @block.scalar
        def _(act):
            def save(i, k, dst):
                n, count = task_bank(i, k)
                act.wait_ge(proj_full[n], count)
                act.activation(dst, proj_ps[n], ACT.Copy).then_inc(proj_saved[n], 1)

            def save_qk(i, k, c):
                save(i, k, qk[:, c].rearrange("p w b t -> p (w b t)"))

            def save_v(i, k, half, b):
                save(i, k, v[:, b, half * 512:half * 512 + 512])

            def exps(i, unit, first, count):
                par = unit % 2
                if first == 0:
                    act.wait_ge(max_ready, i * 4 + (unit + 1))
                for m in range(first, first + count):
                    j, e = m // 2, m % 2
                    act.activation(p[:, par, m, :], s_ps[par][:, e, j, :], ACT.Exp,
                                   bias=neg_max[:, par, 4 * e + j:4 * e + j + 1],
                                   accum_out=p_sum[:, par, m:m + 1]).then_inc(exp_done, 1)

            def body(i, last):
                for j in range(4):
                    save_qk(i, QK1 + j, 4 + j)
                    exps(i, 1, 2 * j, 2)
                save_v(i, V1, 1, 0)
                exps(i, 2, 0, 4)
                save_v(i, V1 + 1, 1, 1)
                exps(i, 2, 4, 4)
                for j in range(4):
                    if not last:
                        save_qk(i, QK0 + j, j)
                    exps(i, 3, 2 * j, 2)
                if not last:
                    save_v(i, V0, 0, 0)
                    exps(i, 4, 0, 4)
                    save_v(i, V0 + 1, 0, 1)
                    exps(i, 4, 4, 4)

            for j in range(4):
                save_qk(-1, QK0 + j, j)
            save_v(-1, V0, 0, 0)
            save_v(-1, V0 + 1, 0, 1)
            exps(0, 0, 0, 8)
            with act.Fori(0, PAIRS - 1) as i:
                body(i, False)
            body(PAIRS - 1, True)

        @block.vector
        def _(dve):
            def ln_moments(i):
                dve.wait_ge(x_loaded, i * 16 + 16)
                for b in range(2):
                    dve.bn_stats(stats[:, b, :], x_in[:, b, :]).then_inc(ln_stats_made, 1)

            def ln_aggregate():
                for b in range(2):
                    dve.bn_aggr(meanvar[:, b, :], stats[:, b, :]).then_inc(ln_stats_made, 1)

            def ln_apply(i):
                dve.wait_ge(ln_rstd_made, i + 1)
                for b in range(2):
                    dve.tensor_scalar(xhat[:, b, :], x_in[:, b, :], meanvar[:, b, 0:1], rstd[:, b:b + 1],
                                      ALU.subtract, ALU.mult).then_inc(xhat_ready, 1)

            def modulate(i):
                n, count = task_bank(i, XT)
                dve.tensor_copy(shsc[:], g.modT[:, bass.ds(i * 2 + 2, 2), :]
                                if not isinstance(i, int) else g.modT[:, 2 * i + 2:2 * i + 4, :]
                                ).then_inc(shsc_ready, 1)
                dve.wait_ge(shsc_ready, i + 2)
                dve.wait_ge(proj_full[n], count)
                for b in range(2):
                    ins = dve.tensor_scalar(xT[:, b, :], proj_ps[n][:, b * T:b * T + T], shsc[:, b, 1:2],
                                            shsc[:, b, 0:1], ALU.mult, ALU.add)
                    ins.then_inc(proj_saved[n] if b else xT_modulated, 1)
                flat = xT[:].rearrange("p b t -> p (b t)")
                dve.wait_ge(proj_saved[n], count)
                dve.tensor_copy(xT_hi[:], flat).then_inc(xT_split, 1)
                dve.wait_ge(xT_split, i * 2 + 3)
                dve.tensor_tensor(xT_lo[:], flat, xT_hi[:].bitcast(F32), ALU.subtract).then_inc(xT_split, 1)

            def row_max(i, unit):
                par = unit % 2
                dve.wait_ge(scores_ready, i * 4 + (unit + 1))
                dve.tensor_reduce(out=neg_max[:, par, :].rearrange("p (e j) -> p e j", e=2), in_=s_ps[par],
                                  op=ALU.max, axis=AX.X, negate=True).then_inc(max_ready, 1)

            def normalise_group(i, unit, grp):
                par = unit % 2
                heads = slice(4 * grp, 4 * grp + 4)
                dve.wait_ge(exp_done, i * 32 + (8 * unit + 4 * grp + 4))
                dve.reciprocal(p_rsum[:, par, heads], p_sum[:, par, heads]).then_inc(rsum_ready, 1)
                dve.wait_ge(rsum_ready, i * 8 + (2 * unit + grp + 1))
                for m in range(4 * grp, 4 * grp + 4):
                    last = dve.tensor_scalar(p[:, par, m, :], p[:, par, m, :], p_rsum[:, par, m:m + 1],
                                             None, ALU.mult)
                last.then_inc(p_ready, 1)

            def normalise(i, unit):
                normalise_group(i, unit, 0)
                normalise_group(i, unit, 1)

            def save_turned(i, unit):
                for grp in range(2):
                    dve.wait_ge(turn_full[grp], i * 8 + (2 * unit + 1) if grp == 0 else i * 4 + (unit + 1))
                    dve.tensor_copy(pT[:, 4 * grp:4 * grp + 4, :].rearrange("p m t -> p (m t)"),
                                    t_ps[grp]).then_inc(turn_saved[grp], 1)

            def save_oT(i, unit):
                half, b = unit // 2, unit % 2
                if half == 0:
                    dve.wait_ge(proj_full[0], i * (TASKS // 2) + 3)
                dve.wait_ge(turn_full[0], i * 8 + (2 * unit + 2))
                dve.tensor_copy(oT[:, b, 4 * half:4 * half + 4, :].rearrange("p c t -> p (c t)"),
                                t_ps[0]).then_inc(turn_saved[0], 1)

            def residual(i):
                n, count = task_bank(i, OUT)
                flat = lambda t: t[:].rearrange("p b f -> p (b f)")
                dve.wait_ge(gate_loaded, i * 16 + 16)
                dve.wait_ge(proj_full[n], count)
                dve.tensor_tensor(flat(gated), proj_ps[n][:, 0:2 * D], flat(gate),
                                  ALU.mult).then_inc(proj_saved[n], 1)
                dve.wait_ge(proj_saved[n], count)
                dve.wait_ge(x_gb_ready, i + 1)
                dve.tensor_tensor(flat(x1), flat(gated), flat(x_gb), ALU.add).then_inc(x1_ready, 1)

            def body(i, last):
                normalise(i, 0)
                save_turned(i, 0)
                save_oT(i, 0)

                row_max(i, 2)
                if not last:
                    ln_moments(i + 1)
                    dve.wait_ge(ln_stats_made, i * 4 + 6)
                normalise_group(i, 1, 0)
                if not last:
                    ln_aggregate()
                normalise_group(i, 1, 1)
                save_turned(i, 1)
                if not last:
                    ln_apply(i + 1)
                save_oT(i, 1)
                if not last:
                    modulate(i)

                row_max(i, 3)
                normalise(i, 2)
                save_turned(i, 2)
                save_oT(i, 2)

                if not last:
                    row_max(i, 4)
                normalise(i, 3)
                save_turned(i, 3)
                save_oT(i, 3)
                if not last:
                    row_max(i, 5)
                residual(i)

            for n in range(2):
                dve.memset(neg_max[:], 0.0).then_inc(turn_saved[n], 1)
                dve.wait_ge(turn_saved[n], 1)
            ln_moments(0)
            dve.wait_ge(ln_stats_made, 2)
            ln_aggregate()
            ln_apply(0)
            modulate(-1)
            row_max(0, 0)
            row_max(0, 1)
            with dve.Fori(0, PAIRS - 1) as i:
                body(i, False)
            body(PAIRS - 1, True)


def step_from(s, k):
    return Step(s.half + (s.par + k) // 2, (s.par + k) % 2)


def run_steps(eng, step):
    step(Step(0, 0), True, False)
    with eng.Fori(0, PAIRS // 2 - 1) as r:
        step(Step(r, 1), False, False)
        step(Step(r + 1, 0), False, False)
    step(Step(PAIRS // 2 - 1, 1), False, True)


def ffn_phase(nc, g):
    with ExitStack() as ctx:
        def sb(name, shape, dt=F32):
            return ctx.enter_context(nc.sbuf_tensor(name, shape, dt))

        def sem(name):
            return ctx.enter_context(nc.semaphore(name))

        def sems(name):
            return [sem(f"{name}{n}") for n in range(2)]

        x_in = sb("f_x_in", [128, 2, 2, D])
        gate = sb("f_gate", [128, 2, 2, D])
        gate_b = sb("f_gate_b2", [128, 2, 2, D])
        x_gb = sb("f_x_gb", [128, 2, 2, D])
        stats = sb("f_stats", [128, 2, 6])
        stats_seen = sb("f_stats_seen", [128, 1])
        meanvar = sb("f_meanvar", [128, 2, 2])
        ln_const = sb("f_ln_const", [128, 2, 2])
        rstd = sb("f_rstd", [128, 2])
        xhat = sb("f_xhat", [128, 2, D])
        shsc = sb("f_shift_scale", [128, 2, COLS])
        xT = sb("f_xT", [128, 2, T])
        xT_hi = sb("f_xT_hi", [128, 2 * T], F32R)
        xT_lo = sb("f_xT_lo", [128, 2 * T], F32R)
        hT = sb("f_hT", [128, 2, MCH, 2 * T])
        gated = sb("f_gated", [128, 2, 2 * D])
        x2 = sb("f_x2", [128, 2, 2, D])

        hid_ps = [g.bank[n][:].rearrange("p (c t) -> p c t", c=MCH) for n in range(2)]
        turn_ps = g.bank[2][:, 0:2 * T]
        out_ps = [g.bank[3][:, 512 * n:512 * n + 2 * D] for n in range(2)]

        x_loaded, gate_loaded, gate_b_loaded = sems("f_x_loaded"), sems("f_gate_loaded"), sems("f_gate_b_loaded")
        stats_made = sem("f_stats_made")
        meanvar_made = sem("f_meanvar_made")
        ln_const_set = sem("f_ln_const_set")
        var_eps = sem("f_var_eps")
        rstd_made = sem("f_rstd_made")
        x_gb_ready = sem("f_x_gb_ready")
        xhat_ready = sem("f_xhat_ready")
        shsc_ready = sem("f_shsc_ready")
        turned = sem("f_turned")
        modulated = sem("f_modulated")
        xT_split = sem("f_xT_split")
        hid_full = sem("f_hid_full")
        gelu_done = sem("f_gelu_done")
        out_full = sem("f_out_full")
        gated_ready = sem("f_gated_ready")
        x2_ready = sem("f_x2_ready")
        x2_stored = sems("f_x2_stored")

        block = ctx.enter_context(nc.Block())

        @block.sync
        def _(sp):
            def load_x(s):
                sp.dma_start(x_in[:, s.par], g.x1_p[s.n]).then_inc(x_loaded[s.par], 16)

            def load_gate_b(s):
                sp.dma_start(gate_b[:, s.par],
                             g.rows_p[s.n][:, 3, :].partition_broadcast(128)).then_inc(gate_b_loaded[s.par], 16)

            def step(s, first, last):
                if not last:
                    sp.wait_ge(x_gb_ready, s.n + 1)
                    sp.wait_ge(xhat_ready, s.n * 2 + 2)
                    load_x(step_from(s, 2))
                    load_gate_b(step_from(s, 2))

            for k in range(2):
                load_x(Step(0, k))
                load_gate_b(Step(0, k))
            step(Step(0, 0), True, False)
            with sp.Fori(0, PAIRS // 2 - 2) as r:
                step(Step(r, 1), False, False)
                step(Step(r + 1, 0), False, False)
            step(Step(PAIRS // 2 - 2, 1), False, False)

        @block.gpsimd
        def _(pool):
            def load_gate(s):
                pool.dma_start(gate[:, s.par],
                               g.rows_p[s.n][:, 2, :].partition_broadcast(128)).then_inc(gate_loaded[s.par], 16)

            def rstd_of(s):
                pool.wait_ge(meanvar_made, s.n * 2 + 2)
                pool.tensor_tensor(rstd[:], meanvar[:, :, 1], ln_const[:, 0], ALU.add).then_inc(var_eps, 1)
                pool.wait_ge(var_eps, s.n + 1)
                pool.tensor_tensor(rstd[:], rstd[:], ln_const[:, 1], ALU.pow).then_inc(rstd_made, 1)

            def store(s):
                pool.wait_ge(x2_ready, s.n + 1)
                pool.dma_start(g.x2_p[s.n], x2[:, s.par]).then_inc(x2_stored[s.par], 16)

            def step(s, first, last):
                if not last:
                    rstd_of(step_from(s, 1))
                pool.wait_ge(gate_loaded[s.par], s.half * 16 + 16)
                pool.wait_ge(x_loaded[s.par], s.half * 16 + 16)
                pool.wait_ge(gate_b_loaded[s.par], s.half * 16 + 16)
                pool.tensor_tensor(x_gb[:, s.par], x_in[:, s.par], gate_b[:, s.par],
                                   ALU.add).then_inc(x_gb_ready, 1)
                if not first:
                    store(step_from(s, -1))
                if not last:
                    load_gate(step_from(s, 1))

            load_gate(Step(0, 0))
            pool.memset(ln_const[:, 0], EPS).then_inc(ln_const_set, 1)
            pool.memset(ln_const[:, 1], -0.5).then_inc(ln_const_set, 1)
            pool.wait_ge(ln_const_set, 2)
            rstd_of(Step(0, 0))
            run_steps(pool, step)
            store(Step(PAIRS // 2 - 1, 1))
            for n in range(2):
                pool.wait_ge(x2_stored[n], PAIRS // 2 * 16)

        @block.tensor
        def _(pe):
            def turn(s):
                pe.wait_ge(xhat_ready, s.n * 2 + 2)
                zero_wait(pe, modulated, s.n * 2)
                for b in range(2):
                    last = pe.transpose(turn_ps[:, b * T:b * T + T], xhat[:, b, :], g.ident[:])
                last.then_inc(turned, 1)

            def hidden(s, first):
                pe.wait_ge(xT_split, s.n * 2 + 2)
                if not first:
                    pe.wait_ge(gelu_done, s.n * 4)
                for c in range(MCH):
                    dst, cols = hid_ps[s.par][:, c, :], slice(c * 128, c * 128 + 128)
                    pe.matmul(dst, g.w1_hi[:, cols], xT_hi[:], start=True, stop=False)
                    pe.matmul(dst, g.w1_hi[:, cols], xT_lo[:], start=False, stop=False)
                    last = pe.matmul(dst, g.w1_lo[:, cols], xT_hi[:], start=False, stop=True)
                    if c % 2:
                        last.then_inc(hid_full, 1)

            def output(s, first):
                pe.wait_ge(gelu_done, s.n * 4 + 4)
                if not first:
                    pe.wait_ge(gated_ready, s.n)
                for b in range(2):
                    for c in range(MCH):
                        last = pe.matmul(out_ps[s.par][:, b * D:b * D + D], hT[:, s.par, c, b * T:b * T + T],
                                         g.w2[:, c, :], start=(c == 0), stop=(c == MCH - 1))
                last.then_inc(out_full, 1)

            def step(s, first, last):
                hidden(s, first)
                if not last:
                    turn(step_from(s, 1))
                if not first:
                    output(step_from(s, -1), False)

            turn(Step(0, 0))
            hidden(Step(0, 0), True)
            turn(Step(0, 1))
            hidden(Step(0, 1), False)
            turn(Step(1, 0))
            output(Step(0, 0), True)
            step(Step(1, 0), False, False)
            with pe.Fori(1, PAIRS // 2 - 1) as r:
                step(Step(r, 1), False, False)
                step(Step(r + 1, 0), False, False)
            step(Step(PAIRS // 2 - 1, 1), False, True)
            output(Step(PAIRS // 2 - 1, 1), False)

        @block.scalar
        def _(act):
            def step(s, first, last):
                for c in range(MCH):
                    if c % 2 == 0:
                        act.wait_ge(hid_full, s.n * 2 + (c // 2 + 1))
                    act.activation(hT[:, s.par, c, :], hid_ps[s.par][:, c, :], ACT.Gelu,
                                   bias=g.b1T[:, c:c + 1]).then_inc(gelu_done, 1)

            run_steps(act, step)

        @block.vector
        def _(dve):
            def layernorm(s):
                dve.wait_ge(x_loaded[s.par], s.half * 16 + 16)
                for b in range(2):
                    dve.bn_stats(stats[:, b, :], x_in[:, s.par, b, :]).then_inc(stats_made, 1)
                dve.wait_ge(stats_made, s.n * 2 + 2)
                dve.memset(stats_seen[:], 0.0)
                for b in range(2):
                    dve.bn_aggr(meanvar[:, b, :], stats[:, b, :]).then_inc(meanvar_made, 1)
                dve.wait_ge(rstd_made, s.n + 1)
                for b in range(2):
                    dve.tensor_scalar(xhat[:, b, :], x_in[:, s.par, b, :], meanvar[:, b, 0:1], rstd[:, b:b + 1],
                                      ALU.subtract, ALU.mult).then_inc(xhat_ready, 1)

            def modulate(s):
                at = bass.ds(s.n * 2, 2) if not isinstance(s.n, int) else slice(2 * s.n, 2 * s.n + 2)
                dve.tensor_copy(shsc[:], g.modT[:, at, :]).then_inc(shsc_ready, 1)
                dve.wait_ge(shsc_ready, s.n + 1)
                dve.wait_ge(turned, s.n + 1)
                for b in range(2):
                    dve.tensor_scalar(xT[:, b, :], turn_ps[:, b * T:b * T + T], shsc[:, b, 3:4],
                                      shsc[:, b, 2:3], ALU.mult, ALU.add).then_inc(modulated, 1)
                flat = xT[:].rearrange("p b t -> p (b t)")
                dve.wait_ge(modulated, s.n * 2 + 2)
                dve.tensor_copy(xT_hi[:], flat).then_inc(xT_split, 1)
                dve.wait_ge(xT_split, s.n * 2 + 1)
                dve.tensor_tensor(xT_lo[:], flat, xT_hi[:].bitcast(F32), ALU.subtract).then_inc(xT_split, 1)

            def residual(s, first):
                flat = lambda t: t.rearrange("p b f -> p (b f)")
                dve.wait_ge(gate_loaded[s.par], s.half * 16 + 16)
                dve.wait_ge(out_full, s.n + 1)
                dve.tensor_tensor(gated[:, s.par], out_ps[s.par], flat(gate[:, s.par]), ALU.mult).then_inc(gated_ready, 1)
                dve.wait_ge(gated_ready, s.n + 1)
                dve.wait_ge(x_gb_ready, s.n + 1)
                if not first:
                    dve.wait_ge(x2_stored[s.par], s.half * 16)
                dve.tensor_tensor(flat(x2[:, s.par]), gated[:, s.par], flat(x_gb[:, s.par]), ALU.add).then_inc(x2_ready, 1)

            def step(s, first, last):
                if not last:
                    layernorm(step_from(s, 1))
                    modulate(step_from(s, 1))
                if not first:
                    residual(step_from(s, -1), False)

            layernorm(Step(0, 0))
            modulate(Step(0, 0))
            step(Step(0, 0), True, False)
            layernorm(Step(1, 0))
            modulate(Step(1, 0))
            residual(Step(0, 0), True)
            layernorm(Step(1, 1))
            modulate(Step(1, 1))
            residual(Step(0, 1), True)
            with dve.Fori(1, PAIRS // 2 - 1) as r:
                step(Step(r, 1), False, False)
                step(Step(r + 1, 0), False, False)
            step(Step(PAIRS // 2 - 1, 1), False, True)
            residual(Step(PAIRS // 2 - 1, 1), False)


def graph_phase(nc, g):
    with ExitStack() as ctx:
        def sb(name, shape, dt=F32):
            return ctx.enter_context(nc.sbuf_tensor(name, shape, dt))

        def sem(name):
            return ctx.enter_context(nc.semaphore(name))

        def sems(name):
            return [sem(f"{name}{n}") for n in range(2)]

        HC = 128 // NG
        KC = HC * NG
        GCH = -(-GH // HC)
        HM = GH * NG
        GW = GD + 1

        x_in = sb("g_x_in", [128, 2, 2, D])
        x_res = sb("g_x_res", [128, 2, 2, D])
        q_row = sb("g_q_row", [128, 2, 2, D])
        a0_raw = sb("g_a0_raw", [128, 2, 2, NG * L], I32)
        a1_raw = sb("g_a1_raw", [2 * NG, 2, T * L], I32)
        a1_f = sb("g_a1_f", [2 * NG, T * L])
        adj = sb("g_adj", [128, 2, 2, NG, L])
        adj_w = sb("g_adj_w", [128, 2, 2, NG, L])
        cond = sb("g_cond", [128, 4 * NG])
        label = sb("g_label", [128, 4 * NG])
        off = sb("g_off", [128, 4 * NG])
        allowed = sb("g_allowed", [128, 2, 4, NG])
        bias = sb("g_bias", [128, 2, 4, NG])
        row_sum = sb("g_row_sum", [128, 2])
        nonzero = sb("g_nonzero", [128, 2])
        self_add = sb("g_self_add", [128, 2, D])
        self_nat = sb("g_self", [128, 2, D])
        self_b = sb("g_self_b", [128, 2, 2, D])
        b_gsum = sb("g_b_sum", [128, D])
        xT = sb("g_xT", [128, 2 * T])
        selfT = sb("g_selfT", [128, 2, T])
        q_bias = sb("g_q_bias", [128, 2])
        qT = sb("g_qT", [128, 2, 2, T])
        kT = sb("g_kT", [128, 2, 2, NG])
        kvT6 = sb("g_kvT6", [128, 2, HC, NG])
        k_block = sb("g_k_block", [128, 4, GH, NG])
        v_mask = sb("g_v_mask", [KC, GH, GD])
        v_block = sb("g_v_block", [KC, 2, 4, GH, GW])
        w = sb("g_w", [128, 2, 2, GH, NG])
        w_max = sb("g_w_max", [128, 2, 2, GH])
        wT = sb("g_wT", [KC, 2, GCH, T])
        r_sum = sb("g_r_sum", [128, 2, 2, GH])
        o = sb("g_o", [128, 2, 2, GH * GD])
        o_sum = sb("g_o_sum", [128, 2, 2, D])
        y = sb("g_y", [128, 2, 2, D])

        aff_ps = [g.bank[n][:].rearrange("p (d c) -> p d c", d=2) for n in range(2)]
        out_ps = [g.bank[n][:, 0:2 * GH * GW].rearrange("p (d h v) -> p d h v", d=2, h=GH) for n in range(2)]
        wT_ps = [g.bank[2][:, 512 * n:512 * n + GCH * T] for n in range(2)]
        misc_ps = [g.bank[3][:, 512 * n:512 * n + 512] for n in range(2)]

        x_loaded, res_loaded, q_row_loaded = sems("g_x_loaded"), sems("g_res_loaded"), sems("g_q_row_loaded")
        a0_loaded, a1_loaded = sems("g_a0_loaded"), sems("g_a1_loaded")
        y_stored = sems("g_y_stored")
        a0_cast = sem("g_a0_cast")
        a1_cast = sem("g_a1_cast")
        weighted = sem("g_weighted")
        adj_summed = sem("g_adj_summed")
        off_ready = sem("g_off_ready")
        bias_ready = sem("g_bias_ready")
        summed = sem("g_summed")
        nonzero_ready = sem("g_nonzero_ready")
        self_add_ready = sem("g_self_add_ready")
        self_b_ready = sem("g_self_b_ready")
        kv6_ready = sem("g_kv6_ready")
        k_block_ready = sem("g_k_block_ready")
        misc_full = sems("g_misc_full")
        misc_saved = sems("g_misc_saved")
        aff_full = sem("g_aff_full")
        masked = sem("g_masked")
        biased = sem("g_biased")
        max_ready = sem("g_max_ready")
        shifted = sem("g_shifted")
        exp_done = sem("g_exp_done")
        wT_full = sems("g_wT_full")
        wT_saved = sems("g_wT_saved")
        out_full = sem("g_out_full")
        r_sum_ready = sem("g_r_sum_ready")
        o_ready = sem("g_o_ready")
        o_added = sem("g_o_added")
        y_ready = sem("g_y_ready")
        consts_set = sem("g_consts_set")
        mask_steps = sem("g_mask_steps")

        XT, SELF, SELFT, ADJ, Q, K, V = range(7)

        def task(s, k):
            m = 7 * s.par + k
            return m % 2, s.half * 7 + (m // 2 + 1)

        def wait_saved(eng, s, k):
            n, count = task(s, k)
            eng.wait_ge(misc_saved[n], count)

        def wait_full(eng, s, k):
            n, count = task(s, k)
            eng.wait_ge(misc_full[n], count)
            return misc_ps[n], misc_saved[n]

        def wait_free(eng, s, k):
            n, count = task(s, k)
            zero_wait(eng, misc_saved[n], count - 1)
            return misc_ps[n], misc_full[n]

        adj_d = g.adj
        zero = Step(0, 0)

        block = ctx.enter_context(nc.Block())

        @block.sync
        def _(sp):
            def load(s):
                sp.dma_start(x_in[:, s.par], g.x2_p[s.n]).then_inc(x_loaded[s.par], 16)
                sp.dma_start(q_row[:, s.par],
                             g.rows_p[s.n][:, 4, :].partition_broadcast(128)).then_inc(q_row_loaded[s.par], 16)
                sp.dma_start(a0_raw[:, s.par],
                             adj_p[s.n][:, :, 0:NG, :].rearrange("b t m l -> t b (m l)")
                             ).then_inc(a0_loaded[s.par], 16)
                for b in range(2):
                    sp.dma_start(a1_raw[b * NG:b * NG + NG, s.par],
                                 adj_p[s.n][b, 0:NG].rearrange("m t l -> m (t l)")).then_inc(a1_loaded[s.par], 16)

            def step(s, first, last):
                sp.wait_ge(a0_cast, s.n + 1)
                sp.wait_ge(a1_cast, s.n + 1)
                sp.wait_ge(self_add_ready, s.n * 2 + 2)
                wait_saved(sp, s, XT)
                load(step_from(s, 2))

            adj_p = adj_d.rearrange("(i b) t m l -> i b t m l", b=2)
            load(zero)
            load(Step(0, 1))
            step(zero, True, False)
            with sp.Fori(0, PAIRS // 2 - 2) as r:
                step(Step(r, 1), False, False)
                step(Step(r + 1, 0), False, False)
            step(Step(PAIRS // 2 - 2, 1), False, False)

        @block.gpsimd
        def _(pool):
            def load_res(s):
                pool.dma_start(x_res[:, s.par], g.x2_p[s.n]).then_inc(res_loaded[s.par], 16)

            def add_bias(s, b):
                pool.wait_ge(masked, s.n * 2 + (b + 1))
                if b == 0:
                    pool.wait_ge(bias_ready, s.n + 1)
                for d in range(2):
                    last = pool.tensor_tensor(w[:, b, d], w[:, b, d],
                                              bias[:, s.par, 2 * d + b, :].unsqueeze(1).broadcast_to([128, GH, NG]),
                                              ALU.add)
                last.then_inc(biased, 1)

            def stage_one(s):
                wait_saved(pool, s, SELF)
                pool.tensor_tensor(self_b[:, s.par], self_nat[:],
                                   b_gsum[:].unsqueeze(1).broadcast_to([128, 2, D]), ALU.add).then_inc(self_b_ready, 1)
                pool.wait_ge(a0_cast, s.n + 1)
                wait_saved(pool, s, ADJ)
                flat = lambda t: t[:].rearrange("p d b m l -> p (d b m) l")
                pool.tensor_tensor(flat(adj_w), flat(adj), g.w_bias[:].unsqueeze(1).broadcast_to([128, 4 * NG, L]),
                                   ALU.mult).then_inc(weighted, 1)
                wait_saved(pool, s, K)
                pool.tensor_tensor(k_block[:], g.blockmask[:].rearrange("p (h m) -> p h m", h=GH).unsqueeze(1)
                                   .broadcast_to([128, 4, GH, NG]),
                                   kT[:].rearrange("p d b m -> p (d b) m").unsqueeze(2)
                                   .broadcast_to([128, 4, GH, NG]), ALU.mult).then_inc(k_block_ready, 1)

            def finish(s):
                pool.wait_ge(o_ready, s.n * 2 + 2)
                pool.tensor_tensor(o_sum[:, s.par], o[:, :, 0, :], o[:, :, 1, :], ALU.add).then_inc(o_added, 1)
                pool.wait_ge(o_added, s.n * 2 + 1)
                pool.tensor_tensor(o_sum[:, s.par], o_sum[:, s.par], self_b[:, s.par], ALU.add).then_inc(o_added, 1)

            def store(s):
                pool.wait_ge(y_ready, s.n + 1)
                pool.dma_start(g.out_p[s.n], y[:, s.par]).then_inc(y_stored[s.par], 16)

            def step(s, first, last):
                add_bias(s, 0)
                add_bias(s, 1)
                if not first:
                    store(step_from(s, -1))
                if not last:
                    load_res(step_from(s, 1))
                    stage_one(step_from(s, 1))
                finish(s)

            load_res(zero)
            pool.memset(v_mask[:], 1.0).then_inc(mask_steps, 1)
            pool.wait_ge(mask_steps, 1)
            steps = 1
            for c in range(GCH):
                heads = min(HC, GH - c * HC)
                part = v_mask[:, c * HC:c * HC + heads, :]
                for base, mult, step_h in ((0, 1, -NG), (NG - 1, -1, NG)):
                    pool.affine_select(out=part, in_=part, compare_op=ALU.is_ge, fill=0.0, base=base,
                                       pattern=[[step_h, heads], [0, GD]], channel_multiplier=mult
                                       ).then_inc(mask_steps, 1)
                    steps += 1
                    pool.wait_ge(mask_steps, steps)
            pool.wait_ge(consts_set, 2)
            stage_one(zero)
            run_steps(pool, step)
            store(Step(PAIRS // 2 - 1, 1))
            for n in range(2):
                pool.wait_ge(y_stored[n], PAIRS // 2 * 16)

        @block.tensor
        def _(pe):
            def turn_x(s):
                pe.wait_ge(x_loaded[s.par], s.half * 16 + 16)
                bank, full = wait_free(pe, s, XT)
                for b in range(2):
                    last = pe.transpose(bank[:, b * T:b * T + T], x_in[:, s.par, b, :], g.ident[:])
                last.then_inc(full, 1)

            def self_features(s):
                wait_saved(pe, s, XT)
                bank, full = wait_free(pe, s, SELF)
                for b in range(2):
                    last = pe.matmul(bank[:, b * D:b * D + D], xT[:, b * T:b * T + T], g.w_self[:, 0, :],
                                     start=True, stop=True)
                last.then_inc(full, 1)

            def turn_self(s):
                pe.wait_ge(a1_cast, s.n + 1)
                wait_saved(pe, s, SELF)
                bank, full = wait_free(pe, s, SELFT)
                for b in range(2):
                    last = pe.transpose(bank[:, b * T:b * T + T], self_nat[:, b, :], g.ident[:])
                last.then_inc(full, 1)

            def turn_adj(s):
                n, _ = task(s, ADJ)
                bank, full = misc_ps[n], misc_full[n]
                by_label = a1_f[:].rearrange("p (t l) -> p t l", l=L)
                for j in range(L):
                    last = pe.transpose(bank[:, j * 2 * NG:j * 2 * NG + 2 * NG], by_label[:, :, j],
                                        g.ident[0:2 * NG, 0:2 * NG])
                last.then_inc(full, 1)

            def queries(s):
                wait_saved(pe, s, SELFT)
                bank, full = wait_free(pe, s, Q)
                for d in range(2):
                    last = pe.matmul(bank[:, d * 2 * T:d * 2 * T + 2 * T], g.gqk_w[:, d, :],
                                     selfT[:].rearrange("p b t -> p (b t)"), start=True, stop=True)
                last.then_inc(full, 1)

            def keys(s):
                wait_saved(pe, s, SELFT)
                bank, full = wait_free(pe, s, K)
                for d in range(2):
                    last = pe.matmul(bank[:, d * 2 * NG:d * 2 * NG + 2 * NG], g.gqk_w[:, 2 + d, :],
                                     selfT[:, :, 0:NG], start=True, stop=True)
                last.then_inc(full, 1)

            def values(s):
                pe.wait_ge(kv6_ready, s.n + 1)
                bank, full = wait_free(pe, s, V)
                for b in range(2):
                    last = pe.matmul(bank[0:KC, b * 256:b * 256 + 256],
                                     kvT6[:, b].rearrange("p h m -> p (h m)"),
                                     g.gout_w[:].rearrange("p d v -> p (d v)"), start=True, stop=True)
                last.then_inc(full, 1)

            def affinity(s, b, first):
                if b == 0:
                    wait_saved(pe, s, Q)
                    pe.wait_ge(k_block_ready, s.n + 1)
                if not first:
                    pe.wait_ge(o_ready, s.n * 2 + (b - 1))
                for d in range(2):
                    last = pe.matmul(aff_ps[b][:, d, 0:HM], qT[:, d, b, :],
                                     k_block[:, 2 * d + b].rearrange("p h m -> p (h m)"), start=True, stop=True)
                last.then_inc(aff_full, 1)

            def turn_w(s, b):
                pe.wait_ge(exp_done, s.n * 2 + (b + 1))
                for d in range(2):
                    zero_wait(pe, wT_saved[d], s.n * 2 + b)
                    flat = w[:, b, d].rearrange("p h m -> p (h m)")
                    for c in range(GCH):
                        rows = min(KC, HM - c * KC)
                        last = pe.transpose(wT_ps[d][0:rows, c * T:c * T + T], flat[:, c * KC:c * KC + rows],
                                            g.ident[:])
                    last.then_inc(wT_full[d], 1)

            def weights_v(s, b):
                wait_saved(pe, s, V)
                for d in range(2):
                    pe.wait_ge(wT_saved[d], s.n * 2 + (b + 1))
                    for c in range(GCH):
                        rows = min(KC, HM - c * KC)
                        heads = slice(c * HC, c * HC + rows // NG)
                        last = pe.matmul(out_ps[b][:, d, heads, :].rearrange("p h v -> p (h v)"),
                                         wT[0:rows, d, c, :],
                                         v_block[0:rows, s.par, 2 * b + d, heads, :].rearrange("p h v -> p (h v)"),
                                         start=True, stop=True)
                last.then_inc(out_full, 1)

            def step(s, first, last):
                nxt = step_from(s, 1)
                if not last:
                    turn_x(nxt)
                    self_features(nxt)
                turn_w(s, 0)
                if not last:
                    turn_self(nxt)
                weights_v(s, 0)
                if not last:
                    turn_adj(nxt)
                    queries(nxt)
                    keys(nxt)
                turn_w(s, 1)
                if not last:
                    values(nxt)
                weights_v(s, 1)
                if not last:
                    affinity(nxt, 0, False)
                    affinity(nxt, 1, False)

            for stage in (turn_x, self_features, turn_self, turn_adj, queries, keys, values):
                stage(zero)
            affinity(zero, 0, True)
            affinity(zero, 1, True)
            run_steps(pe, step)

        @block.scalar
        def _(act):
            def save(s, k, dst, view=lambda t: t):
                src, saved = wait_full(act, s, k)
                act.activation(dst, view(src), ACT.Copy).then_inc(saved, 1)

            def casts(s):
                act.wait_ge(a0_loaded[s.par], s.half * 16 + 16)
                zero_wait(act, adj_summed, s.n * 2)
                act.activation(adj[:, 0].rearrange("p b m l -> p b (m l)"), a0_raw[:, s.par],
                               ACT.Copy).then_inc(a0_cast, 1)
                act.wait_ge(a1_loaded[s.par], s.half * 32 + 32)
                act.activation(a1_f[:], a1_raw[:, s.par], ACT.Copy).then_inc(a1_cast, 1)

            def save_xT(s):
                save(s, XT, xT[:], lambda t: t[:, 0:2 * T])

            def save_selfT(s):
                save(s, SELFT, selfT[:].rearrange("p b t -> p (b t)"), lambda t: t[:, 0:2 * T])
                wait_saved(act, s, SELFT)
                act.activation(kvT6[:], selfT[:, :, 0:NG].unsqueeze(2).broadcast_to([128, 2, HC, NG]),
                               ACT.Copy).then_inc(kv6_ready, 1)

            def save_adj(s):
                save(s, ADJ, adj[:, 1].rearrange("p b m l -> p l (b m)"),
                     lambda t: t[:, 0:L * 2 * NG].rearrange("p (l r) -> p l r", l=L))

            def save_q(s):
                src, saved = wait_full(act, s, Q)
                for d in range(2):
                    last = act.activation(qT[:, d].rearrange("p b t -> p (b t)"), src[:, d * 2 * T:d * 2 * T + 2 * T],
                                          ACT.Identity, bias=q_bias[:, d:d + 1], scale=GSCALE)
                last.then_inc(saved, 1)

            def weights(s, b):
                act.wait_ge(shifted, s.n * 2 + (b + 1))
                flat = w[:, b].rearrange("p d h m -> p (d h m)")
                act.activation(flat, flat, ACT.Exp).then_inc(exp_done, 1)

            def save_wT(s, b):
                for d in range(2):
                    act.wait_ge(wT_full[d], s.n * 2 + (b + 1))
                    full_rows = HM // KC
                    act.activation(wT[:, d, 0:full_rows, :].rearrange("p c t -> p (c t)"),
                                   wT_ps[d][0:KC, 0:full_rows * T], ACT.Copy)
                    rest = HM - full_rows * KC
                    act.activation(wT[0:rest, d, full_rows, :], wT_ps[d][0:rest, full_rows * T:GCH * T],
                                   ACT.Copy).then_inc(wT_saved[d], 1)

            def step(s, first, last):
                nxt = step_from(s, 1)
                if not last:
                    casts(nxt)
                    save_xT(nxt)
                weights(s, 0)
                save_wT(s, 0)
                if not last:
                    save_selfT(nxt)
                    save_adj(nxt)
                    save_q(nxt)
                weights(s, 1)
                save_wT(s, 1)

            casts(zero)
            act.wait_ge(consts_set, 2)
            save_xT(zero)
            save_selfT(zero)
            save_adj(zero)
            save_q(zero)
            run_steps(act, step)

        @block.vector
        def _(dve):
            def self_terms(s):
                dve.wait_ge(x_loaded[s.par], s.half * 16 + 16)
                dve.reduce_sum(row_sum[:], x_in[:, s.par], AX.X).then_inc(summed, 1)
                dve.wait_ge(summed, s.n + 1)
                dve.tensor_scalar(nonzero[:], row_sum[:], 0.0, None, ALU.not_equal).then_inc(nonzero_ready, 1)
                dve.wait_ge(nonzero_ready, s.n + 1)
                dve.wait_ge(q_row_loaded[s.par], s.half * 16 + 16)
                for b in range(2):
                    dve.scalar_tensor_tensor(out=self_add[:, b, :], in0=q_row[:, s.par, b, :],
                                             scalar=nonzero[:, b:b + 1], in1=g.b_self[:], op0=ALU.mult,
                                             op1=ALU.add).then_inc(self_add_ready, 1)

            def save_self(s):
                dve.wait_ge(self_add_ready, s.n * 2 + 2)
                zero_wait(dve, self_b_ready, s.n)
                src, saved = wait_full(dve, s, SELF)
                dve.tensor_tensor(self_nat[:], src[:, 0:2 * D].rearrange("p (b f) -> p b f", b=2), self_add[:],
                                  ALU.add).then_inc(saved, 1)

            def mask_and_bias(s):
                dve.wait_ge(weighted, s.n + 1)
                flat = lambda t: t[:].rearrange("p d b m l -> p (d b m) l")
                dve.reduce_sum(label[:], flat(adj_w), AX.X).then_inc(adj_summed, 1)
                dve.reduce_sum(cond[:], flat(adj), AX.X).then_inc(adj_summed, 1)
                dve.wait_ge(adj_summed, s.n * 2 + 2)
                dve.tensor_scalar(allowed[:, s.par].rearrange("p r m -> p (r m)"), cond[:], 0.0, None,
                                  ALU.is_gt).then_inc(off_ready, 1)
                dve.tensor_scalar(off[:], cond[:], 0.0, NEG, ALU.is_le, ALU.mult).then_inc(off_ready, 1)
                dve.wait_ge(off_ready, s.n * 2 + 2)
                dve.scalar_tensor_tensor(out=bias[:, s.par].rearrange("p r m -> p (r m)"), in0=label[:],
                                         scalar=g.b_bias[:], in1=off[:], op0=ALU.add,
                                         op1=ALU.add).then_inc(bias_ready, 1)

            def save_k(s):
                src, saved = wait_full(dve, s, K)
                for d in range(2):
                    last = dve.tensor_scalar(kT[:, d].rearrange("p b m -> p (b m)"),
                                             src[:, d * 2 * NG:d * 2 * NG + 2 * NG],
                                             g.gqk_b[:, 2 + d:3 + d], None, ALU.add)
                last.then_inc(saved, 1)

            def save_v(s):
                src, saved = wait_full(dve, s, V)
                dve.tensor_tensor(v_block[:, s.par, :, :, 0:GD],
                                  src[0:KC, :].rearrange("p (r h v) -> p r h v", r=4, h=GH),
                                  v_mask[:].unsqueeze(1).broadcast_to([KC, 4, GH, GD]), ALU.mult).then_inc(saved, 1)

            def mask_scores(s, b):
                dve.wait_ge(aff_full, s.n * 2 + (b + 1))
                if b == 0:
                    dve.wait_ge(off_ready, s.n * 2 + 2)
                for d in range(2):
                    last = dve.tensor_tensor(w[:, b, d], aff_ps[b][:, d, 0:HM].rearrange("p (h m) -> p h m", h=GH),
                                             allowed[:, s.par, 2 * d + b, :].unsqueeze(1)
                                             .broadcast_to([128, GH, NG]), ALU.mult)
                last.then_inc(masked, 1)

            def shift_scores(s, b):
                rows = w[:, b].rearrange("p d h m -> p (d h) m")
                dve.wait_ge(biased, s.n * 2 + (b + 1))
                dve.reduce_max(w_max[:, b].rearrange("p d h -> p (d h)"), rows, AX.X).then_inc(max_ready, 1)
                dve.wait_ge(max_ready, s.n * 2 + (b + 1))
                dve.tensor_tensor(rows, rows, w_max[:, b].rearrange("p d h -> p (d h)").unsqueeze(2)
                                  .broadcast_to([128, 2 * GH, NG]), ALU.subtract).then_inc(shifted, 1)

            def save_out(s, b):
                dve.wait_ge(out_full, s.n * 2 + (b + 1))
                dve.reciprocal(r_sum[:, b], out_ps[b][:, :, :, GD]).then_inc(r_sum_ready, 1)
                dve.wait_ge(r_sum_ready, s.n * 2 + (b + 1))
                if b == 0:
                    zero_wait(dve, o_added, s.n * 2)
                dve.tensor_tensor(o[:, b].rearrange("p d (h v) -> p d h v", h=GH), out_ps[b][:, :, :, 0:GD],
                                  r_sum[:, b].unsqueeze(3).broadcast_to([128, 2, GH, GD]),
                                  ALU.mult).then_inc(o_ready, 1)

            def finish(s):
                dve.wait_ge(o_added, s.n * 2 + 2)
                dve.wait_ge(res_loaded[s.par], s.half * 16 + 16)
                zero_wait(dve, y_stored[s.par], s.half * 16)
                flat = lambda t: t[:, s.par].rearrange("p b f -> p (b f)")
                dve.scalar_tensor_tensor(out=flat(y), in0=flat(o_sum), scalar=0.0, in1=flat(x_res), op0=ALU.max,
                                         op1=ALU.add).then_inc(y_ready, 1)

            def step(s, first, last):
                nxt = step_from(s, 1)
                mask_scores(s, 0)
                mask_scores(s, 1)
                if not last:
                    self_terms(nxt)
                shift_scores(s, 0)
                shift_scores(s, 1)
                if not first:
                    finish(step_from(s, -1))
                if not last:
                    save_self(nxt)
                    mask_and_bias(nxt)
                    save_k(nxt)
                save_out(s, 0)
                if not last:
                    save_v(nxt)
                save_out(s, 1)

            dve.tensor_scalar(q_bias[:], g.gqk_b[:, 0:2], GSCALE, None, ALU.mult).then_inc(consts_set, 1)
            dve.tensor_tensor(b_gsum[:], g.b_gout[:, 0:D], g.b_gout[:, D:2 * D], ALU.add).then_inc(consts_set, 1)
            self_terms(zero)
            save_self(zero)
            mask_and_bias(zero)
            save_k(zero)
            dve.wait_ge(mask_steps, 1 + 2 * GCH)
            for n in range(2):
                dve.tensor_copy(v_block[:, n, :, :, GD],
                                v_mask[:, :, 0].unsqueeze(1).broadcast_to([KC, 4, GH]))
            save_v(zero)
            step(zero, True, False)
            step(Step(0, 1), False, False)
            step(Step(1, 0), False, False)
            with dve.Fori(1, PAIRS // 2 - 1) as r:
                step(Step(r, 1), False, False)
                step(Step(r + 1, 0), False, False)
            step(Step(PAIRS // 2 - 1, 1), False, True)
            finish(Step(PAIRS // 2 - 1, 1))


def build(nc, a):
    with ExitStack() as ctx:
        def sb(name, shape, dt=F32):
            return ctx.enter_context(nc.sbuf_tensor(name, shape, dt))

        g = Kept()
        g.rows_d = nc.dram_tensor("rows_scratch", (B, ROWS, D), F32, kind="Internal").ap()
        x1_d = nc.dram_tensor("x1_scratch", (B, T, D), F32, kind="Internal").ap()
        x2_d = nc.dram_tensor("x2_scratch", (B, T, D), F32, kind="Internal").ap()

        def of_pairs(t):
            return t.rearrange("(i b) t f -> i t b f", b=2)

        g.x_p, g.x1_p, g.x2_p, g.out_p = of_pairs(a["x"]), of_pairs(x1_d), of_pairs(x2_d), of_pairs(a["out"])
        g.rows_p = g.rows_d.rearrange("(i b) r f -> i b r f", b=2)
        g.adj = a["mask"]

        g.ident = sb("ident", [128, 128])
        g.modT = sb("modT", [128, B, COLS])
        g.wq_hi = sb("w_qkv_hi", [128, 3 * INNER], F32R)
        g.wq_lo = sb("w_qkv_lo", [128, 3 * INNER], F32R)
        g.w_out = sb("w_out_sb", [128, CHUNKS, D])
        g.w1_hi = sb("w1_hi", [128, MLP], F32R)
        g.w1_lo = sb("w1_lo", [128, MLP], F32R)
        g.b1T = sb("b1T_sb", [128, MCH])
        g.w2 = sb("w2_sb", [128, MCH, D])
        g.w_self = sb("w_self_sb", [128, 2, D])
        g.b_self = sb("b_self_sb", [128, D])
        g.gqk_w = sb("gqk_w", [128, 4, D])
        g.gqk_b = sb("gqk_b", [128, 4])
        g.gout_w = sb("gout_w", [128, 2, GH * GD])
        g.b_gout = sb("b_gout_sb", [128, 2 * D])
        g.w_bias = sb("w_bias_sb", [128, L])
        g.b_bias = sb("b_bias_sb", [128, 1])
        g.blockmask = sb("blockmask", [128, GH * NG])
        g.bank = [ctx.enter_context(nc.psum_tensor(f"banks{n}", [128, 1024], F32)) for n in range(4)]

        setup_phase(nc, g, a)
        attention_phase(nc, g)
        ffn_phase(nc, g)
        graph_phase(nc, g)


def kernel(**inputs):
    import numpy as _np
    import concourse.bacc as _bacc
    from concourse import mybir as _mybir
    from concourse.bass_utils import run_bass_kernel_spmd as _run

    nc = _bacc.Bacc("TRN2", target_bir_lowering=False, num_devices=1)
    t = {k: _np.asarray(v) for k, v in inputs.items()}
    gqk = _np.stack([t["L1_cond_Wq"][0], t["L1_cond_Wq"][1], t["L1_cond_Wk"][0], t["L1_cond_Wk"][1]])
    gb = _np.stack([t["L1_cond_bq"][0], t["L1_cond_bq"][1], t["L1_cond_bk"][0], t["L1_cond_bk"][1]])
    laid = {
        "x": t["x"], "cT": t["cond_1024"].T, "mask": t["mask_BxSxSx11_ik0"],
        "w_mod": t["L0_cond_W_mod"], "b_mod": t["L0_cond_b_mod"],
        "b_modT": t["L0_cond_b_mod"].reshape(6, D).T,
        "w_qkv": t["L0_cond_W_qkv"], "w_out": t["L0_cond_W_out"], "b_out": t["L0_cond_b_out"],
        "w1": t["L0_cond_W1"], "b1T": t["L0_cond_b1"].reshape(MCH, 128).T,
        "w2": t["L0_cond_W2"], "b2": t["L0_cond_b2"],
        "w_selfT": t["L1_cond_W_self"].T, "b_self": t["L1_cond_b_self"],
        "w_bias": t["L1_cond_w_bias"], "b_bias": t["L1_cond_b_bias"].reshape(1),
        "gqkT": gqk.transpose(2, 0, 1), "gbT": gb.T,
        "w_goutT": t["L1_cond_Wout"].transpose(3, 0, 1, 2).reshape(D, 2, GH * GD),
        "b_gout": t["L1_cond_bout"].reshape(2 * D),
        "blockmask": _np.kron(_np.eye(GH), _np.ones((GD, NG))).astype(_np.float32),
    }
    arrays, a = {}, {}
    for name, value in laid.items():
        value = _np.ascontiguousarray(value)
        arrays[f"in_{name}"] = value
        ap = nc.dram_tensor(f"in_{name}", value.shape, _mybir.dt.from_np(value.dtype), kind="ExternalInput").ap()
        a[name] = ap
    a["out"] = nc.dram_tensor("out_0", (B, T, D), F32, kind="ExternalOutput").ap()
    build(nc, a)
    r = _run(nc, [arrays], core_ids=[0])
    return r.results[0]["out_0"]
```
